# Optimizing a Trainium2 kernel written in Bass

```python
import numpy as np
import jax
import jax.numpy as jnp

def _softmax(x, axis=-1):
    return jax.nn.softmax(x, axis=axis)

def _gelu(x):
    return jax.nn.gelu(x, approximate=True)

def _silu(x):
    return jax.nn.silu(x)

def _sigmoid(x):
    return jax.nn.sigmoid(x)

def _layernorm(x, axis=-1, eps=1e-05):
    m = jnp.mean(x, axis=axis, keepdims=True)
    v = jnp.var(x, axis=axis, keepdims=True)
    return (x - m) / jnp.sqrt(v + eps)

def _scatter_add(tgt, idx, src, axis=0):
    return tgt.at[idx].add(src)

def _segment_sum(src, seg, n):
    return jax.ops.segment_sum(src, seg, n)
kernel_name = 'mk_dlrm_tower_d1_rec_r8_9e8956'

def setup_inputs(seed: int=0):
    np.random.seed(seed)
    _w = jnp.asarray

    def _rec_inputs():
        import jax
        import jax.numpy as jnp
        _tk = jax.random.key(seed)
        dense_ctx = jax.random.normal(jax.random.fold_in(_tk, 190), (512, 16), jnp.float32)
        ids = jnp.stack([jax.random.randint(jax.random.fold_in(_tk, 200 + f), (512,), 0, v, jnp.int32) for f, v in enumerate([1000, 1000, 125000, 1250, 1000, 12500, 1250, 1250, 1000, 12500, 1000, 1250, 1250, 1250, 1000, 1000, 1000, 1000, 12500, 12500, 1000, 1250, 1250, 1250, 12500, 12500, 1000])], axis=1)
        tbl_0 = 0.05 * jax.random.normal(jax.random.fold_in(_tk, 500 + 0), (1000, 128), jnp.float32)
        tbl_1 = 0.05 * jax.random.normal(jax.random.fold_in(_tk, 500 + 1), (1000, 128), jnp.float32)
        tbl_2 = 0.05 * jax.random.normal(jax.random.fold_in(_tk, 500 + 2), (125000, 128), jnp.float32)
        tbl_3 = 0.05 * jax.random.normal(jax.random.fold_in(_tk, 500 + 3), (1250, 128), jnp.float32)
        tbl_4 = 0.05 * jax.random.normal(jax.random.fold_in(_tk, 500 + 4), (1000, 128), jnp.float32)
        tbl_5 = 0.05 * jax.random.normal(jax.random.fold_in(_tk, 500 + 5), (12500, 128), jnp.float32)
        tbl_6 = 0.05 * jax.random.normal(jax.random.fold_in(_tk, 500 + 6), (1250, 128), jnp.float32)
        tbl_7 = 0.05 * jax.random.normal(jax.random.fold_in(_tk, 500 + 7), (1250, 128), jnp.float32)
        tbl_8 = 0.05 * jax.random.normal(jax.random.fold_in(_tk, 500 + 8), (1000, 128), jnp.float32)
        tbl_9 = 0.05 * jax.random.normal(jax.random.fold_in(_tk, 500 + 9), (12500, 128), jnp.float32)
        tbl_10 = 0.05 * jax.random.normal(jax.random.fold_in(_tk, 500 + 10), (1000, 128), jnp.float32)
        tbl_11 = 0.05 * jax.random.normal(jax.random.fold_in(_tk, 500 + 11), (1250, 128), jnp.float32)
        tbl_12 = 0.05 * jax.random.normal(jax.random.fold_in(_tk, 500 + 12), (1250, 128), jnp.float32)
        tbl_13 = 0.05 * jax.random.normal(jax.random.fold_in(_tk, 500 + 13), (1250, 128), jnp.float32)
        tbl_14 = 0.05 * jax.random.normal(jax.random.fold_in(_tk, 500 + 14), (1000, 128), jnp.float32)
        tbl_15 = 0.05 * jax.random.normal(jax.random.fold_in(_tk, 500 + 15), (1000, 128), jnp.float32)
        tbl_16 = 0.05 * jax.random.normal(jax.random.fold_in(_tk, 500 + 16), (1000, 128), jnp.float32)
        tbl_17 = 0.05 * jax.random.normal(jax.random.fold_in(_tk, 500 + 17), (1000, 128), jnp.float32)
        tbl_18 = 0.05 * jax.random.normal(jax.random.fold_in(_tk, 500 + 18), (12500, 128), jnp.float32)
        tbl_19 = 0.05 * jax.random.normal(jax.random.fold_in(_tk, 500 + 19), (12500, 128), jnp.float32)
        tbl_20 = 0.05 * jax.random.normal(jax.random.fold_in(_tk, 500 + 20), (1000, 128), jnp.float32)
        tbl_21 = 0.05 * jax.random.normal(jax.random.fold_in(_tk, 500 + 21), (1250, 128), jnp.float32)
        tbl_22 = 0.05 * jax.random.normal(jax.random.fold_in(_tk, 500 + 22), (1250, 128), jnp.float32)
        tbl_23 = 0.05 * jax.random.normal(jax.random.fold_in(_tk, 500 + 23), (1250, 128), jnp.float32)
        tbl_24 = 0.05 * jax.random.normal(jax.random.fold_in(_tk, 500 + 24), (12500, 128), jnp.float32)
        tbl_25 = 0.05 * jax.random.normal(jax.random.fold_in(_tk, 500 + 25), (12500, 128), jnp.float32)
        tbl_26 = 0.05 * jax.random.normal(jax.random.fold_in(_tk, 500 + 26), (1000, 128), jnp.float32)
        _rk = jax.random.fold_in(_tk, 7)
        W_top1 = 0.0161733 * jax.random.normal(jax.random.fold_in(_tk, 801), (3823, 512), jnp.float32)
        W_top2 = 0.0441942 * jax.random.normal(jax.random.fold_in(_tk, 802), (512, 256), jnp.float32)
        W_top3 = 0.0625 * jax.random.normal(jax.random.fold_in(_tk, 803), (256, 1), jnp.float32)
        b_top1 = jnp.zeros((512,), jnp.float32)
        b_top2 = jnp.zeros((256,), jnp.float32)
        return (dense_ctx, ids, tbl_0, tbl_1, tbl_2, tbl_3, tbl_4, tbl_5, tbl_6, tbl_7, tbl_8, tbl_9, tbl_10, tbl_11, tbl_12, tbl_13, tbl_14, tbl_15, tbl_16, tbl_17, tbl_18, tbl_19, tbl_20, tbl_21, tbl_22, tbl_23, tbl_24, tbl_25, tbl_26, W_top1, b_top1, W_top2, b_top2, W_top3)
    dense_ctx, ids, tbl_0, tbl_1, tbl_2, tbl_3, tbl_4, tbl_5, tbl_6, tbl_7, tbl_8, tbl_9, tbl_10, tbl_11, tbl_12, tbl_13, tbl_14, tbl_15, tbl_16, tbl_17, tbl_18, tbl_19, tbl_20, tbl_21, tbl_22, tbl_23, tbl_24, tbl_25, tbl_26, W_top1, b_top1, W_top2, b_top2, W_top3 = _rec_inputs()

    def _L0_rec_setup():
        import jax, jax.numpy as jnp
        import numpy as np
        NUM_FEATURES = 27
        FEATURE_DIM = 128
        BATCH = 2048
        _TRIU_I, _TRIU_J = np.triu_indices(NUM_FEATURES, k=1)
        key = jax.random.key(seed)
        embeddings = jax.random.normal(key, (BATCH, NUM_FEATURES, FEATURE_DIM), dtype=jnp.float32)
        return {'embeddings': embeddings}
    _L0_rec_all = _L0_rec_setup()
    _L0_rec_in = {k: v for k, v in _L0_rec_all.items() if k in ()}
    del _L0_rec_all
    return {'dense_ctx': dense_ctx, 'ids': ids, 'tbl_0': tbl_0, 'tbl_1': tbl_1, 'tbl_2': tbl_2, 'tbl_3': tbl_3, 'tbl_4': tbl_4, 'tbl_5': tbl_5, 'tbl_6': tbl_6, 'tbl_7': tbl_7, 'tbl_8': tbl_8, 'tbl_9': tbl_9, 'tbl_10': tbl_10, 'tbl_11': tbl_11, 'tbl_12': tbl_12, 'tbl_13': tbl_13, 'tbl_14': tbl_14, 'tbl_15': tbl_15, 'tbl_16': tbl_16, 'tbl_17': tbl_17, 'tbl_18': tbl_18, 'tbl_19': tbl_19, 'tbl_20': tbl_20, 'tbl_21': tbl_21, 'tbl_22': tbl_22, 'tbl_23': tbl_23, 'tbl_24': tbl_24, 'tbl_25': tbl_25, 'tbl_26': tbl_26, 'W_top1': W_top1, 'b_top1': b_top1, 'W_top2': W_top2, 'b_top2': b_top2, 'W_top3': W_top3}

def reference(dense_ctx, ids, tbl_0, tbl_1, tbl_2, tbl_3, tbl_4, tbl_5, tbl_6, tbl_7, tbl_8, tbl_9, tbl_10, tbl_11, tbl_12, tbl_13, tbl_14, tbl_15, tbl_16, tbl_17, tbl_18, tbl_19, tbl_20, tbl_21, tbl_22, tbl_23, tbl_24, tbl_25, tbl_26, W_top1, b_top1, W_top2, b_top2, W_top3):
    import jax
    import jax.numpy as jnp

    def _L0_rec_ref(embeddings):
        import jax, jax.numpy as jnp
        import numpy as np
        NUM_FEATURES = 27
        FEATURE_DIM = 128
        BATCH = 2048
        _TRIU_I, _TRIU_J = np.triu_indices(NUM_FEATURES, k=1)
        B = embeddings.shape[0]
        interactions = jnp.einsum('bfd,bgd->bfg', embeddings, embeddings)
        flat_interactions = interactions[:, _TRIU_I, _TRIU_J]
        flat_embeddings = embeddings.reshape(B, -1)
        return jnp.concatenate([flat_embeddings, flat_interactions], axis=1)
    e = jnp.stack([tbl_0[ids[:, 0]], tbl_1[ids[:, 1]], tbl_2[ids[:, 2]], tbl_3[ids[:, 3]], tbl_4[ids[:, 4]], tbl_5[ids[:, 5]], tbl_6[ids[:, 6]], tbl_7[ids[:, 7]], tbl_8[ids[:, 8]], tbl_9[ids[:, 9]], tbl_10[ids[:, 10]], tbl_11[ids[:, 11]], tbl_12[ids[:, 12]], tbl_13[ids[:, 13]], tbl_14[ids[:, 14]], tbl_15[ids[:, 15]], tbl_16[ids[:, 16]], tbl_17[ids[:, 17]], tbl_18[ids[:, 18]], tbl_19[ids[:, 19]], tbl_20[ids[:, 20]], tbl_21[ids[:, 21]], tbl_22[ids[:, 22]], tbl_23[ids[:, 23]], tbl_24[ids[:, 24]], tbl_25[ids[:, 25]], tbl_26[ids[:, 26]]], axis=1)
    z = _L0_rec_ref(e)
    z = z.reshape(z.shape[0], -1)
    h = jnp.concatenate([z, dense_ctx], axis=1)
    h = jnp.maximum(h @ W_top1 + b_top1, 0.0)
    h = jnp.maximum(h @ W_top2 + b_top2, 0.0)
    y = h @ W_top3
    return y

_drawn_inputs = setup_inputs


def setup_inputs(seed=0):
    import zlib

    import numpy as np

    out = dict(_drawn_inputs(seed))
    spreads = {'b_top1': (0.0, 0.1), 'b_top2': (0.0, 0.1)}
    factors = {}
    for name, (base, spread) in spreads.items():
        noise = np.random.default_rng([zlib.crc32(name.encode()), seed]).standard_normal(out[name].shape)
        drawn = base * np.exp(spread * noise) if base else spread * noise
        out[name] = jnp.asarray(drawn.astype(out[name].dtype))
    for name, factor in factors.items():
        out[name] = (out[name] * factor).astype(out[name].dtype)
    return out
```

```python
import concourse.bass as bass
from concourse import mybir
from contextlib import ExitStack


def dlrm_tower(nc, dense_ctx, ids, tables, W_top1, b_top1, W_top2, b_top2, W_top3, y_out):
    f32, f32r, i32 = mybir.dt.float32, mybir.dt.float32r, mybir.dt.int32
    ALU = mybir.AluOpType
    ACT = mybir.ActivationFunctionType

    P = 128
    B, F = ids.shape
    D = tables[0].shape[1]
    CTX = dense_ctx.shape[1]
    H1, H2 = W_top2.shape
    NT = B // P
    QF = 4
    NQ = -(-F // QF)
    RING = 15
    SPG = 4
    ROWS = P // SPG
    NG = P // SPG
    HG = NG // 2
    GSTEP = 128
    NF = F - 1
    CI = -(-NF // 4)
    CW = F + CI
    STAGE = 3
    CTX_AT = (NF - 4 * (CI - 1)) * ROWS
    K_LAST = CTX_AT + ROWS
    PAIR0 = F * D
    CTX0 = PAIR0 + F * (F - 1) // 2
    HC = H1 // P
    MC = H2 // P
    assert B == NT * P and D == P and CTX < ROWS and H1 == 512 and F <= ROWS

    def pair_row(f):
        return PAIR0 + f * (F - 1) - f * (f - 1) // 2

    def quad_features(q):
        return range(QF * q, min(QF * q + QF, F))

    ctx = ExitStack()
    with ctx:
        def sb(name, shape, dt):
            return ctx.enter_context(nc.sbuf_tensor(name, shape, dt))

        def sem(name):
            return ctx.enter_context(nc.semaphore(name))

        w_hi = sb("w_hi", [P, CW, H1], f32r)
        w_lo = sb("w_lo", [P, CW, H1], f32r)
        e_hi = sb("e_hi", [P, 2, P, ROWS], f32r)
        e_lo = sb("e_lo", [P, 2, P, ROWS], f32r)
        g_hi = sb("g_hi", [P, CI, P], f32r)
        g_lo = sb("g_lo", [P, CI, P], f32r)
        rows = sb("rows", [P, RING, D], f32)
        stage = sb("stage", [P, STAGE, H1], f32)
        h1 = stage[:, 0, :]
        h1T = stage[:, 0, :].rearrange("p (c b) -> p c b", c=HC)
        h2T = stage[:, 0, 0:MC * P].rearrange("p (m b) -> p m b", m=MC)
        y_row = stage[0:1, 0, MC * P:MC * P + P]
        w2 = stage[:, 1:3, :].rearrange("p a (c n) -> p (a c) n", n=H2)
        ids_sb = sb("ids_sb", [P, NT, F], i32)
        ctx_sb = sb("ctx_sb", [P, NT, CTX], f32)
        b2 = sb("b2", [P, MC], f32)
        w3 = sb("w3", [P, MC], f32)
        ident = sb("ident", [P, P], f32)

        h1_ps = [ctx.enter_context(nc.psum_tensor(f"h1_ps{i}", [P, H1], f32)) for i in range(2)]
        tp_ps = [ctx.enter_context(nc.psum_tensor(f"tp_ps{i}", [P, QF, P], f32)) for i in range(2)]
        gram_ps = ctx.enter_context(nc.psum_tensor("gram_ps", [P, 4 * 512], f32))
        h1T_ps = gram_ps[:, 0:HC * P]
        h2_ps = gram_ps[:, 512:512 + MC * P].rearrange("p (m b) -> p m b", m=MC)
        y_ps = gram_ps[0:1, 1024:1024 + P]

        ids0_loaded = sem("ids0_loaded")
        ids_loaded = sem("ids_loaded")
        ctx_loaded = sem("ctx_loaded")
        ident_zeroed = sem("ident_zeroed")
        ident_ready = sem("ident_ready")
        pads_ready = sem("pads_ready")
        rows_landed = [sem(f"rows_landed{i}") for i in range(RING)]
        w_landed = [sem(f"w_landed{i}") for i in range(STAGE)]
        stage_zeroed = sem("stage_zeroed")
        w_hi_ready = sem("w_hi_ready")
        w_lo_ready = sem("w_lo_ready")
        small_loaded = sem("small_loaded")
        transposed = sem("transposed")
        e_hi_ready = sem("e_hi_ready")
        e_lo_ready = sem("e_lo_ready")
        gram_done = sem("gram_done")
        g_hi_ready = sem("g_hi_ready")
        g_lo_ready = sem("g_lo_ready")
        h1_done = sem("h1_done")
        h1_ready = sem("h1_ready")
        h1_transposed = sem("h1_transposed")
        h1T_ready = sem("h1T_ready")
        h2_done = sem("h2_done")
        h2_ready = sem("h2_ready")
        y_done = sem("y_done")
        y_ready = sem("y_ready")
        y_stored = sem("y_stored")

        def samples(e, t, f0, f1):
            return e[:, t % 2, :, f0:f1].rearrange("p b f -> p f b")

        def w_dmas(c):
            return 1 if c < F else 4

        def w_count(c):
            return 16 * sum(w_dmas(i) for i in range(c % STAGE, c + 1, STAGE))

        def w_chunks_with(k):
            if k < NQ:
                return list(quad_features(k))
            after = k - NQ
            return [c for c in range(F, CW) if min((c - F) // 3, 2) == after]

        def evac_parts():
            for j in range(SPG):
                for q in range(4):
                    yield j, q, len(range(q, NF, 4))

        def gram_view(half, j, q, n):
            v = gram_ps[ROWS * j:ROWS * j + F, :].rearrange("p (g x) -> p x g", x=GSTEP)
            return v[:, j * NF + q:j * NF + q + 4 * (n - 1) + 1:4, :]

        def pair_view(g, half, j, q, n):
            v = g[ROWS * q:ROWS * q + F, 0:n, :].rearrange("p c (g s) -> p c g s", s=SPG)
            return v[:, :, half * HG:(half + 1) * HG, j]

        block = ctx.enter_context(nc.Block())

        @block.sync
        def _(sp):
            ids_v = ids.rearrange("(t p) f -> p t f", p=P)
            sp.dma_start(ids_sb[:, 0, :], ids_v[:, 0, :]).then_inc(ids0_loaded, 16)
            for c in range(F):
                if c >= STAGE:
                    sp.wait_ge(w_lo_ready, c - STAGE + 1)
                sp.dma_start(stage[:, c % STAGE, :], W_top1[c * D:(c + 1) * D, :]).then_inc(w_landed[c % STAGE], 16)
                if c == 1:
                    sp.dma_start(ids_sb[:, 1:NT, :], ids_v[:, 1:NT, :]).then_inc(ids_loaded, 16)
                    sp.dma_start(ctx_sb[:, :, :], dense_ctx.rearrange("(t p) f -> p t f", p=P)).then_inc(ctx_loaded, 16)
            for c in range(F, CW):
                slot = stage[:, c % STAGE, :]
                sp.wait_ge(stage_zeroed, c - F + 1)
                for q in range(4):
                    f = 4 * (c - F) + q
                    if f < NF:
                        n = F - 1 - f
                        sp.dma_start(slot[ROWS * q + f + 1:ROWS * q + F, :],
                                     W_top1[pair_row(f):pair_row(f) + n, :]).then_inc(w_landed[c % STAGE], 16)
                if c == CW - 1:
                    sp.dma_start(slot[CTX_AT:CTX_AT + CTX, :],
                                 W_top1[CTX0:CTX0 + CTX, :]).then_inc(w_landed[c % STAGE], 16)
                    sp.dma_start(slot[CTX_AT + CTX:CTX_AT + CTX + 1, :],
                                 b_top1.rearrange("(a n) -> a n", a=1)).then_inc(w_landed[c % STAGE], 16)
            sp.wait_ge(w_lo_ready, CW)
            sp.dma_start(w2, W_top2.rearrange("(c p) n -> p c n", p=P)).then_inc(small_loaded, 16)
            with nc.allow_non_contiguous_dma(reason="256 values"):
                sp.dma_start(b2[:, :], b_top2.rearrange("(m p) -> p m", p=P)).then_inc(small_loaded, 16)
                sp.dma_start(w3[:, :], W_top3.rearrange("(m p) o -> p (m o)", p=P)).then_inc(small_loaded, 16)
            for t in range(NT):
                sp.wait_ge(y_ready, t + 1)
                sp.dma_start(y_out[t * P:(t + 1) * P, :].rearrange("p o -> o p"), y_row).then_inc(y_stored, 16)
            sp.wait_ge(y_stored, 16 * NT)

        @block.gpsimd
        def _(pool):
            nc.gpsimd.memset(ident[:, :], 0.0).then_inc(ident_zeroed, 1)
            pool.wait_ge(ident_zeroed, 1)
            nc.gpsimd.affine_select(out=ident[:, :], in_=ident[:, :], compare_op=ALU.not_equal, fill=1.0,
                                    base=0, pattern=[[-1, P]], channel_multiplier=1).then_inc(ident_ready, 1)
            for k in range(NT * NQ):
                t, q = divmod(k, NQ)
                if k == 0:
                    pool.wait_ge(ids0_loaded, 16)
                if k == NQ:
                    pool.wait_ge(ids_loaded, 16)
                for f in quad_features(q):
                    n = t * F + f
                    if n >= RING:
                        old_t, old_f = divmod(n - RING, F)
                        pool.wait_ge(transposed, old_t * NQ + old_f // QF + 1)
                    nc.gpsimd.indirect_dma_start(
                        rows[:, n % RING, :], None, tables[f],
                        bass.IndirectOffsetOnAxis(ids_sb[:, t, f:f + 1], 0)).then_inc(rows_landed[n % RING], 16)

        @block.scalar
        def _(act):
            def split_w(c):
                act.wait_ge(w_landed[c % STAGE], w_count(c))
                nc.scalar.activation(w_hi[:, c, :], stage[:, c % STAGE, :], ACT.Copy).then_inc(w_hi_ready, 1)

            def split_e(t, q):
                k = t * NQ + q
                for c in w_chunks_with(k):
                    split_w(c)
                if q == 0 and t >= 2:
                    act.wait_ge(gram_done, 2 * (t - 1))
                act.wait_ge(transposed, k + 1)
                fs = quad_features(q)
                last = nc.scalar.activation(samples(e_hi, t, fs[0], fs[-1] + 1), tp_ps[k % 2][:, 0:len(fs), :], ACT.Copy)
                if q == NQ - 1:
                    if t >= 1:
                        act.wait_ge(h1_done, t)
                    else:
                        act.wait_ge(pads_ready, 1)
                    last = nc.scalar.activation(g_hi[CTX_AT:CTX_AT + CTX, CI - 1, :],
                                                tp_ps[k % 2][0:CTX, QF - 1, :], ACT.Copy)
                last.then_inc(e_hi_ready, 1)

            def split_gram(t, half):
                act.wait_ge(gram_done, 2 * t + half + 1)
                if half == 0 and t >= 1:
                    act.wait_ge(h1_done, t)
                if half == 0 and t == 0:
                    act.wait_ge(pads_ready, 1)
                for j, q, n in evac_parts():
                    last = nc.scalar.activation(pair_view(g_hi, half, j, q, n), gram_view(half, j, q, n), ACT.Copy)
                    if q == 3:
                        last.then_inc(g_hi_ready, 1)

            def relu_h1(t):
                act.wait_ge(h1_done, t + 1)
                if t == 0:
                    act.wait_ge(w_lo_ready, CW)
                else:
                    act.wait_ge(y_stored, 16 * t)
                nc.scalar.activation(h1, h1_ps[t % 2][:, :], ACT.Relu).then_inc(h1_ready, 1)

            def relu_h2(t):
                act.wait_ge(h2_done, t + 1)
                if t == 0:
                    act.wait_ge(small_loaded, 48)
                for m in range(MC):
                    last = nc.scalar.activation(h2T[:, m, :], h2_ps[:, m, :], ACT.Relu, bias=b2[:, m:m + 1])
                last.then_inc(h2_ready, 1)

            split_e(0, 0)
            for t in range(NT + 1):
                if t < NT:
                    split_e(t, 1)
                if t >= 1:
                    split_gram(t - 1, 0)
                if t < NT:
                    split_e(t, 2)
                    split_e(t, 3)
                if t >= 1:
                    split_gram(t - 1, 1)
                if t < NT:
                    split_e(t, 4)
                if t >= 1:
                    relu_h1(t - 1)
                if t < NT:
                    split_e(t, 5)
                    split_e(t, 6)
                if t >= 1:
                    relu_h2(t - 1)
                if t + 1 < NT:
                    split_e(t + 1, 0)

        @block.vector
        def _(dve):
            def split_w(c):
                dve.wait_ge(w_hi_ready, c + 1)
                nc.vector.tensor_tensor(w_lo[:, c, :], stage[:, c % STAGE, :], w_hi[:, c, :],
                                        ALU.subtract).then_inc(w_lo_ready, 1)
                if F <= c + STAGE < CW:
                    dve.wait_ge(w_lo_ready, c + 1)
                    nc.vector.memset(stage[:, c % STAGE, :], 0.0).then_inc(stage_zeroed, 1)

            def split_e(t, q):
                k = t * NQ + q
                for c in w_chunks_with(k):
                    split_w(c)
                dve.wait_ge(e_hi_ready, k + 1)
                fs = quad_features(q)
                last = nc.vector.tensor_tensor(samples(e_lo, t, fs[0], fs[-1] + 1), tp_ps[k % 2][:, 0:len(fs), :],
                                               samples(e_hi, t, fs[0], fs[-1] + 1), ALU.subtract)
                if q == NQ - 1:
                    last = nc.vector.tensor_tensor(g_lo[CTX_AT:CTX_AT + CTX, CI - 1, :],
                                                   tp_ps[k % 2][0:CTX, QF - 1, :],
                                                   g_hi[CTX_AT:CTX_AT + CTX, CI - 1, :], ALU.subtract)
                last.then_inc(e_lo_ready, 1)

            def split_gram(t, half):
                for j, q, n in evac_parts():
                    if q == 0:
                        dve.wait_ge(g_hi_ready, SPG * (2 * t + half) + j + 1)
                    last = nc.vector.tensor_tensor(pair_view(g_lo, half, j, q, n), gram_view(half, j, q, n),
                                                   pair_view(g_hi, half, j, q, n), ALU.subtract)
                last.then_inc(g_lo_ready, 1)

            def copy_h1T(t):
                dve.wait_ge(h1_transposed, t + 1)
                nc.vector.tensor_copy(h1T, h1T_ps.rearrange("p (c b) -> p c b", c=HC)).then_inc(h1T_ready, 1)

            def copy_y(t):
                dve.wait_ge(y_done, t + 1)
                nc.vector.tensor_copy(y_row, y_ps).then_inc(y_ready, 1)

            nc.vector.memset(e_hi[:, :, :, F:ROWS].bitcast(f32), 0.0)
            nc.vector.memset(e_lo[:, :, :, F:ROWS].bitcast(f32), 0.0)
            nc.vector.memset(g_hi[:, :, :].bitcast(f32), 0.0).then_inc(pads_ready, 1)
            nc.vector.memset(g_lo[:, :, :].bitcast(f32), 0.0)
            dve.wait_ge(pads_ready, 1)
            nc.vector.memset(g_hi[CTX_AT:K_LAST, CI - 1, :].bitcast(f32), 1.0).then_inc(pads_ready, 1)

            split_e(0, 0)
            for t in range(NT + 1):
                if t < NT:
                    split_e(t, 1)
                if t >= 1:
                    split_gram(t - 1, 0)
                if t < NT:
                    split_e(t, 2)
                    split_e(t, 3)
                if t >= 1:
                    split_gram(t - 1, 1)
                if t < NT:
                    split_e(t, 4)
                    split_e(t, 5)
                if t >= 1:
                    copy_h1T(t - 1)
                if t < NT:
                    split_e(t, 6)
                if t + 1 < NT:
                    split_e(t + 1, 0)
                if t >= 1:
                    copy_y(t - 1)

        @block.tensor
        def _(pe):
            def transposes(t, q):
                k = t * NQ + q
                if k == 0:
                    pe.wait_ge(ident_ready, 1)
                if k >= 2:
                    pe.wait_ge(e_lo_ready, k - 1)
                for i, f in enumerate(quad_features(q)):
                    n = t * F + f
                    pe.wait_ge(rows_landed[n % RING], 16 * (n // RING + 1))
                    last = nc.tensor.transpose(tp_ps[k % 2][:, i, :], rows[:, n % RING, :], ident[:, :])
                if q == NQ - 1:
                    if t == 0:
                        pe.wait_ge(ctx_loaded, 16)
                    last = nc.tensor.transpose(tp_ps[k % 2][0:CTX, QF - 1, :], ctx_sb[:, t, :], ident[:, :])
                last.then_inc(transposed, 1)

            def product(out, hi, lo, whi, wlo, start, stop):
                nc.tensor.matmul(out, hi, whi, start=start, stop=False)
                nc.tensor.matmul(out, hi, wlo, start=False, stop=False)
                return nc.tensor.matmul(out, lo, whi, start=False, stop=stop)

            def embeddings_h1(t, q):
                if q == 0 and t >= 2:
                    pe.wait_ge(h1_ready, t - 1)
                pe.wait_ge(e_lo_ready, t * NQ + q + 1)
                for f in quad_features(q):
                    if t == 0:
                        pe.wait_ge(w_lo_ready, f + 1)
                    product(h1_ps[t % 2][:, :], e_hi[:, t % 2, :, f], e_lo[:, t % 2, :, f],
                            w_hi[:, f, :], w_lo[:, f, :], f == 0, False)

            def gram(t, half):
                if t == 0 and half == 0:
                    pe.wait_ge(pads_ready, 2)
                if half == 1:
                    pe.wait_ge(g_lo_ready, 2 * t + 1)
                for g in range(HG):
                    if half == 0 and g == HG // 2 and t >= 1:
                        pe.wait_ge(y_ready, t)
                    b = SPG * (half * HG + g)
                    out = gram_ps[:, g * GSTEP:g * GSTEP + NF * SPG]
                    hi, lo = e_hi[:, t % 2, b:b + SPG, :], e_lo[:, t % 2, b:b + SPG, :]
                    last = product(out, hi.rearrange("p s f -> p (s f)"), lo.rearrange("p s f -> p (s f)"),
                                   hi[:, :, 0:NF], lo[:, :, 0:NF], True, True)
                last.then_inc(gram_done, 1)

            def pairs_h1(t):
                pe.wait_ge(g_lo_ready, 2 * t + 2)
                for c in range(CI):
                    if t == 0:
                        pe.wait_ge(w_lo_ready, F + c + 1)
                    k = P if c < CI - 1 else K_LAST
                    last = product(h1_ps[t % 2][:, :], g_hi[0:k, c, :], g_lo[0:k, c, :],
                                   w_hi[0:k, F + c, :], w_lo[0:k, F + c, :], False, c == CI - 1)
                last.then_inc(h1_done, 1)

            def transpose_h1(t):
                pe.wait_ge(h1_ready, t + 1)
                for c in range(HC):
                    last = nc.tensor.transpose(h1T_ps[:, c * P:(c + 1) * P], h1[:, c * P:(c + 1) * P], ident[:, :])
                last.then_inc(h1_transposed, 1)

            def layer2(t):
                pe.wait_ge(h1T_ready, t + 1)
                if t == 0:
                    pe.wait_ge(small_loaded, 48)
                for m in range(MC):
                    for c in range(HC):
                        last = nc.tensor.matmul(h2_ps[:, m, :], w2[:, c, m * P:(m + 1) * P], h1T[:, c, :],
                                                start=c == 0, stop=c == HC - 1)
                last.then_inc(h2_done, 1)

            def layer3(t):
                pe.wait_ge(h2_ready, t + 1)
                for m in range(MC):
                    last = nc.tensor.matmul(y_ps, w3[:, m:m + 1], h2T[:, m, :], start=m == 0, stop=m == MC - 1)
                last.then_inc(y_done, 1)

            transposes(0, 0)
            for t in range(NT + 1):
                if t < NT:
                    transposes(t, 1)
                    embeddings_h1(t, 0)
                    transposes(t, 2)
                    embeddings_h1(t, 1)
                if t >= 1:
                    gram(t - 1, 1)
                if t < NT:
                    transposes(t, 3)
                    embeddings_h1(t, 2)
                    transposes(t, 4)
                    embeddings_h1(t, 3)
                if t >= 1:
                    pairs_h1(t - 1)
                if t < NT:
                    transposes(t, 5)
                    embeddings_h1(t, 4)
                if t >= 1:
                    transpose_h1(t - 1)
                if t < NT:
                    transposes(t, 6)
                    embeddings_h1(t, 5)
                if t >= 1:
                    layer2(t - 1)
                if t + 1 < NT:
                    transposes(t + 1, 0)
                if t < NT:
                    embeddings_h1(t, 6)
                if t >= 1:
                    layer3(t - 1)
                if t < NT:
                    gram(t, 0)


_TABLES = [f"tbl_{f}" for f in range(27)]
_INS = ["dense_ctx", "ids"] + _TABLES + ["W_top1", "b_top1", "W_top2", "b_top2", "W_top3"]


def kernel(**inputs):
    import numpy as _np
    import concourse.bacc as _bacc
    from concourse import mybir as _mybir
    from concourse.bass_utils import run_bass_kernel_spmd as _run

    nc = _bacc.Bacc("TRN2", target_bir_lowering=False, num_devices=1, dynamic_dma_scratch_size=2048)
    arrays, aps = {}, {}
    for name in _INS:
        a = _np.ascontiguousarray(inputs[name])
        arrays[f"in_{name}"] = a
        aps[name] = nc.dram_tensor(f"in_{name}", a.shape, _mybir.dt.from_np(a.dtype), kind="ExternalInput").ap()
    y = nc.dram_tensor("out_y", (aps["ids"].shape[0], 1), _mybir.dt.from_np(_np.dtype("float32")),
                       kind="ExternalOutput").ap()
    dlrm_tower(nc, aps["dense_ctx"], aps["ids"], [aps[n] for n in _TABLES], aps["W_top1"], aps["b_top1"],
               aps["W_top2"], aps["b_top2"], aps["W_top3"], y)
    return _run(nc, [arrays], core_ids=[0]).results[0]["out_y"]
```

```python
import concourse.bass as bass
from concourse import mybir
from contextlib import ExitStack


def dlrm_tower(nc, dense_ctx, ids, tables, W_top1, b_top1, W_top2, b_top2, W_top3, y_out):
    f32, f32r, i32 = mybir.dt.float32, mybir.dt.float32r, mybir.dt.int32
    ALU = mybir.AluOpType
    ACT = mybir.ActivationFunctionType

    P = 128
    B, F = ids.shape
    D = tables[0].shape[1]
    CTX = dense_ctx.shape[1]
    H1, H2 = W_top2.shape
    NT = B // P
    QF = 4
    NQ = -(-F // QF)
    RING = 24
    SPG = 4
    ROWS = P // SPG
    NG = P // SPG
    HG = NG // 2
    GSTEP = 128
    NF = F - 1
    CI = -(-NF // 4)
    CW = F + CI
    STAGE = 8
    PER_DMA = 2
    ER = 3
    CTX_AT = (NF - 4 * (CI - 1)) * ROWS
    K_LAST = CTX_AT + ROWS
    PAIR0 = F * D
    CTX0 = PAIR0 + F * (F - 1) // 2
    HC = H1 // P
    MC = H2 // P
    assert B == NT * P and D == P and CTX < ROWS and H1 == 512 and F <= ROWS

    def pair_row(f):
        return PAIR0 + f * (F - 1) - f * (f - 1) // 2

    def quad_features(q):
        return range(QF * q, min(QF * q + QF, F))

    ctx = ExitStack()
    with ctx:
        def sb(name, shape, dt):
            return ctx.enter_context(nc.sbuf_tensor(name, shape, dt))

        def sem(name):
            return ctx.enter_context(nc.semaphore(name))

        w_hi = sb("w_hi", [P, CW, H1], f32r)
        w_lo = sb("w_lo", [P, CW, H1], f32r)
        e_raw = sb("e_raw", [P, 2, P, ROWS], f32)
        e_hi = sb("e_hi", [P, ER, QF, P], f32r)
        e_lo = sb("e_lo", [P, ER, QF, P], f32r)
        g_hi = sb("g_hi", [P, CI, P], f32r)
        g_lo = sb("g_lo", [P, CI, P], f32r)
        rows = sb("rows", [P, RING, D], f32)
        stage = sb("stage", [P, STAGE, H1], f32)
        h1 = stage[:, 0, :]
        h1T = stage[:, 0, :].rearrange("p (c b) -> p c b", c=HC)
        h2T = stage[:, 0, 0:MC * P].rearrange("p (m b) -> p m b", m=MC)
        y_row = stage[0:1, 0, MC * P:MC * P + P]
        w2 = stage[:, 1:3, :].rearrange("p a (c n) -> p (a c) n", n=H2)
        ids_sb = sb("ids_sb", [P, NT, F], i32)
        ctx_sb = sb("ctx_sb", [P, NT, CTX], f32)
        b2 = sb("b2", [P, MC], f32)
        w3 = sb("w3", [P, MC], f32)
        ident = sb("ident", [P, P], f32)

        h1_ps = [ctx.enter_context(nc.psum_tensor(f"h1_ps{i}", [P, H1], f32)) for i in range(2)]
        tp_ps = [ctx.enter_context(nc.psum_tensor(f"tp_ps{i}", [P, QF, P], f32)) for i in range(2)]
        gram_ps = ctx.enter_context(nc.psum_tensor("gram_ps", [P, 4 * 512], f32))
        h1T_ps = gram_ps[:, 0:HC * P]
        h2_ps = gram_ps[:, 512:512 + MC * P].rearrange("p (m b) -> p m b", m=MC)
        y_ps = gram_ps[0:1, 1024:1024 + P]

        ids0_loaded = sem("ids0_loaded")
        ids_loaded = sem("ids_loaded")
        ctx_loaded = sem("ctx_loaded")
        ident_zeroed = sem("ident_zeroed")
        ident_ready = sem("ident_ready")
        pads_ready = sem("pads_ready")
        rows_landed = [sem(f"rows_landed{i}") for i in range(RING)]
        w_landed = [sem(f"w_landed{i}") for i in range(STAGE)]
        stage_zeroed = sem("stage_zeroed")
        w_hi_ready = sem("w_hi_ready")
        w_lo_ready = sem("w_lo_ready")
        small_loaded = sem("small_loaded")
        transposed = sem("transposed")
        e_raw_ready = sem("e_raw_ready")
        e_hi_ready = sem("e_hi_ready")
        e_used = sem("e_used")
        e_lo_ready = sem("e_lo_ready")
        gram_done = sem("gram_done")
        g_hi_ready = sem("g_hi_ready")
        g_lo_ready = sem("g_lo_ready")
        h1_done = sem("h1_done")
        h1_ready = sem("h1_ready")
        h1_transposed = sem("h1_transposed")
        h1T_ready = sem("h1T_ready")
        h2_done = sem("h2_done")
        h2_ready = sem("h2_ready")
        y_done = sem("y_done")
        y_ready = sem("y_ready")
        y_stored = sem("y_stored")

        def w_dmas(c):
            if c < F:
                return 1 if c % PER_DMA == 0 else 0
            return 4

        def w_sem(c):
            return w_landed[c % STAGE if c >= F else c % STAGE // PER_DMA * PER_DMA]

        def w_count(c):
            return 16 * sum(w_dmas(i) for i in range(c + 1) if w_sem(i) is w_sem(c))

        def w_chunks_with(k):
            if k < NQ:
                return list(quad_features(k))
            after = k - NQ
            return [c for c in range(F, CW) if min((c - F) // 3, 2) == after]

        def evac_parts():
            for j in range(SPG):
                for q in range(4):
                    yield j, q, len(range(q, NF, 4))

        def gram_view(half, j, q, n):
            v = gram_ps[ROWS * j:ROWS * j + F, :].rearrange("p (g x) -> p x g", x=GSTEP)
            return v[:, j * NF + q:j * NF + q + 4 * (n - 1) + 1:4, :]

        def pair_view(g, half, j, q, n):
            v = g[ROWS * q:ROWS * q + F, 0:n, :].rearrange("p c (g s) -> p c g s", s=SPG)
            return v[:, :, half * HG:(half + 1) * HG, j]

        block = ctx.enter_context(nc.Block())

        @block.sync
        def _(sp):
            ids_v = ids.rearrange("(t p) f -> p t f", p=P)
            sp.dma_start(ids_sb[:, 0, :], ids_v[:, 0, :]).then_inc(ids0_loaded, 16)
            for c in range(0, F, PER_DMA):
                n = min(PER_DMA, F - c)
                if c >= STAGE:
                    sp.wait_ge(w_lo_ready, c + n - STAGE)
                sp.dma_start(stage[:, c % STAGE:c % STAGE + n, :],
                             W_top1[c * D:(c + n) * D, :].rearrange("(c p) n -> p c n", p=P)).then_inc(w_sem(c), 16)
                if c == 0:
                    sp.dma_start(ids_sb[:, 1:NT, :], ids_v[:, 1:NT, :]).then_inc(ids_loaded, 16)
                    sp.dma_start(ctx_sb[:, :, :], dense_ctx.rearrange("(t p) f -> p t f", p=P)).then_inc(ctx_loaded, 16)
            for c in range(F, CW):
                slot = stage[:, c % STAGE, :]
                sp.wait_ge(stage_zeroed, c - F + 1)
                for q in range(4):
                    f = 4 * (c - F) + q
                    if f < NF:
                        n = F - 1 - f
                        sp.dma_start(slot[ROWS * q + f + 1:ROWS * q + F, :],
                                     W_top1[pair_row(f):pair_row(f) + n, :]).then_inc(w_sem(c), 16)
                if c == CW - 1:
                    sp.dma_start(slot[CTX_AT:CTX_AT + CTX, :],
                                 W_top1[CTX0:CTX0 + CTX, :]).then_inc(w_sem(c), 16)
                    sp.dma_start(slot[CTX_AT + CTX:CTX_AT + CTX + 1, :],
                                 b_top1.rearrange("(a n) -> a n", a=1)).then_inc(w_sem(c), 16)
            sp.wait_ge(w_lo_ready, CW)
            sp.dma_start(w2, W_top2.rearrange("(c p) n -> p c n", p=P)).then_inc(small_loaded, 16)
            with nc.allow_non_contiguous_dma(reason="256 values"):
                sp.dma_start(b2[:, :], b_top2.rearrange("(m p) -> p m", p=P)).then_inc(small_loaded, 16)
                sp.dma_start(w3[:, :], W_top3.rearrange("(m p) o -> p (m o)", p=P)).then_inc(small_loaded, 16)
            for t in range(NT):
                sp.wait_ge(y_ready, t + 1)
                sp.dma_start(y_out[t * P:(t + 1) * P, :].rearrange("p o -> o p"), y_row).then_inc(y_stored, 16)
            sp.wait_ge(y_stored, 16 * NT)

        @block.gpsimd
        def _(pool):
            nc.gpsimd.memset(ident[:, :], 0.0).then_inc(ident_zeroed, 1)
            pool.wait_ge(ident_zeroed, 1)
            nc.gpsimd.affine_select(out=ident[:, :], in_=ident[:, :], compare_op=ALU.not_equal, fill=1.0,
                                    base=0, pattern=[[-1, P]], channel_multiplier=1).then_inc(ident_ready, 1)
            for k in range(NT * NQ):
                t, q = divmod(k, NQ)
                if k == 0:
                    pool.wait_ge(ids0_loaded, 16)
                if k == NQ:
                    pool.wait_ge(ids_loaded, 16)
                for f in quad_features(q):
                    n = t * F + f
                    if n >= RING:
                        old_t, old_f = divmod(n - RING, F)
                        pool.wait_ge(transposed, old_t * NQ + old_f // QF + 1)
                    nc.gpsimd.indirect_dma_start(
                        rows[:, n % RING, :], None, tables[f],
                        bass.IndirectOffsetOnAxis(ids_sb[:, t, f:f + 1], 0)).then_inc(rows_landed[n % RING], 16)

        @block.scalar
        def _(act):
            def split_w(c):
                act.wait_ge(w_sem(c), w_count(c))
                nc.scalar.activation(w_hi[:, c, :], stage[:, c % STAGE, :], ACT.Copy).then_inc(w_hi_ready, 1)

            def split_e(t, q):
                k = t * NQ + q
                for c in w_chunks_with(k):
                    split_w(c)
                fs = quad_features(q)
                if q == 0 and t == 0:
                    act.wait_ge(pads_ready, 3)
                if q == 0 and t >= 2:
                    act.wait_ge(gram_done, 2 * (t - 1))
                act.wait_ge(transposed, k + 1)
                nc.scalar.activation(e_raw[:, t % 2, :, fs[0]:fs[-1] + 1].rearrange("p b f -> p f b"),
                                     tp_ps[k % 2][:, 0:len(fs), :], ACT.Copy).then_inc(e_raw_ready, 1)
                if k >= ER:
                    act.wait_ge(e_used, k - ER + 1)
                last = nc.scalar.activation(e_hi[:, k % ER, 0:len(fs), :], tp_ps[k % 2][:, 0:len(fs), :], ACT.Copy)
                if q == NQ - 1:
                    if t >= 1:
                        act.wait_ge(h1_done, t)
                    last = nc.scalar.activation(g_hi[CTX_AT:CTX_AT + CTX, CI - 1, :],
                                                tp_ps[k % 2][0:CTX, QF - 1, :], ACT.Copy)
                last.then_inc(e_hi_ready, 1)

            def split_gram(t, half):
                act.wait_ge(gram_done, 2 * t + half + 1)
                if half == 0 and t >= 1:
                    act.wait_ge(h1_done, t)
                for j, q, n in evac_parts():
                    last = nc.scalar.activation(pair_view(g_hi, half, j, q, n), gram_view(half, j, q, n), ACT.Copy)
                    if q == 3:
                        last.then_inc(g_hi_ready, 1)

            def relu_h1(t):
                act.wait_ge(h1_done, t + 1)
                if t == 0:
                    act.wait_ge(w_lo_ready, CW)
                else:
                    act.wait_ge(y_stored, 16 * t)
                nc.scalar.activation(h1, h1_ps[t % 2][:, :], ACT.Relu).then_inc(h1_ready, 1)

            def relu_h2(t):
                act.wait_ge(h2_done, t + 1)
                if t == 0:
                    act.wait_ge(small_loaded, 48)
                for m in range(MC):
                    last = nc.scalar.activation(h2T[:, m, :], h2_ps[:, m, :], ACT.Relu, bias=b2[:, m:m + 1])
                last.then_inc(h2_ready, 1)

            split_e(0, 0)
            for t in range(NT + 1):
                if t >= 1:
                    split_gram(t - 1, 0)
                if t < NT:
                    split_e(t, 1)
                    split_e(t, 2)
                if t >= 1:
                    split_gram(t - 1, 1)
                if t < NT:
                    split_e(t, 3)
                    split_e(t, 4)
                if t >= 1:
                    relu_h1(t - 1)
                if t < NT:
                    split_e(t, 5)
                    split_e(t, 6)
                if t >= 1:
                    relu_h2(t - 1)
                if t + 1 < NT:
                    split_e(t + 1, 0)

        @block.vector
        def _(dve):
            def split_w(c):
                dve.wait_ge(w_hi_ready, c + 1)
                nc.vector.tensor_tensor(w_lo[:, c, :], stage[:, c % STAGE, :], w_hi[:, c, :],
                                        ALU.subtract).then_inc(w_lo_ready, 1)
                if F <= c + STAGE < CW:
                    dve.wait_ge(w_lo_ready, c + 1)
                    nc.vector.memset(stage[:, c % STAGE, :], 0.0).then_inc(stage_zeroed, 1)

            def split_e(t, q):
                k = t * NQ + q
                for c in w_chunks_with(k):
                    split_w(c)
                dve.wait_ge(e_hi_ready, k + 1)
                fs = quad_features(q)
                last = nc.vector.tensor_tensor(e_lo[:, k % ER, 0:len(fs), :], tp_ps[k % 2][:, 0:len(fs), :],
                                               e_hi[:, k % ER, 0:len(fs), :], ALU.subtract)
                if q == NQ - 1:
                    last = nc.vector.tensor_tensor(g_lo[CTX_AT:CTX_AT + CTX, CI - 1, :],
                                                   tp_ps[k % 2][0:CTX, QF - 1, :],
                                                   g_hi[CTX_AT:CTX_AT + CTX, CI - 1, :], ALU.subtract)
                last.then_inc(e_lo_ready, 1)

            def split_gram(t, half):
                for j, q, n in evac_parts():
                    if q == 0:
                        dve.wait_ge(g_hi_ready, SPG * (2 * t + half) + j + 1)
                    last = nc.vector.tensor_tensor(pair_view(g_lo, half, j, q, n), gram_view(half, j, q, n),
                                                   pair_view(g_hi, half, j, q, n), ALU.subtract)
                last.then_inc(g_lo_ready, 1)

            def copy_h1T(t):
                dve.wait_ge(h1_transposed, t + 1)
                nc.vector.tensor_copy(h1T, h1T_ps.rearrange("p (c b) -> p c b", c=HC)).then_inc(h1T_ready, 1)

            def copy_y(t):
                dve.wait_ge(y_done, t + 1)
                nc.vector.tensor_copy(y_row, y_ps).then_inc(y_ready, 1)

            nc.vector.memset(e_raw[:, :, :, F:ROWS], 0.0).then_inc(pads_ready, 1)
            nc.vector.memset(g_hi[:, :, :].bitcast(f32), 0.0).then_inc(pads_ready, 1)
            dve.wait_ge(pads_ready, 2)
            nc.vector.memset(g_hi[CTX_AT:K_LAST, CI - 1, :].bitcast(f32), 1.0).then_inc(pads_ready, 1)
            nc.vector.memset(g_lo[:, :, :].bitcast(f32), 0.0)

            split_e(0, 0)
            for t in range(NT + 1):
                if t >= 1:
                    split_gram(t - 1, 0)
                if t < NT:
                    split_e(t, 1)
                    split_e(t, 2)
                if t >= 1:
                    split_gram(t - 1, 1)
                if t < NT:
                    split_e(t, 3)
                    split_e(t, 4)
                    split_e(t, 5)
                if t >= 1:
                    copy_h1T(t - 1)
                if t < NT:
                    split_e(t, 6)
                if t + 1 < NT:
                    split_e(t + 1, 0)
                if t >= 1:
                    copy_y(t - 1)

        @block.tensor
        def _(pe):
            def transposes(t, q):
                k = t * NQ + q
                if k == 0:
                    pe.wait_ge(ident_ready, 1)
                if k >= 2:
                    pe.wait_ge(e_lo_ready, k - 1)
                for i, f in enumerate(quad_features(q)):
                    n = t * F + f
                    pe.wait_ge(rows_landed[n % RING], 16 * (n // RING + 1))
                    last = nc.tensor.transpose(tp_ps[k % 2][:, i, :], rows[:, n % RING, :], ident[:, :])
                if q == NQ - 1:
                    if t == 0:
                        pe.wait_ge(ctx_loaded, 16)
                    last = nc.tensor.transpose(tp_ps[k % 2][0:CTX, QF - 1, :], ctx_sb[:, t, :], ident[:, :])
                last.then_inc(transposed, 1)

            def product(out, hi, lo, whi, wlo, start, stop):
                nc.tensor.matmul(out, hi, whi, start=start, stop=False)
                nc.tensor.matmul(out, hi, wlo, start=False, stop=False)
                return nc.tensor.matmul(out, lo, whi, start=False, stop=stop)

            def embeddings_h1(t, q):
                if q == 0 and t >= 2:
                    pe.wait_ge(h1_ready, t - 1)
                k = t * NQ + q
                pe.wait_ge(e_lo_ready, k + 1)
                for f in quad_features(q):
                    if t == 0:
                        pe.wait_ge(w_lo_ready, f + 1)
                    last = product(h1_ps[t % 2][:, :], e_hi[:, k % ER, f - QF * q, :], e_lo[:, k % ER, f - QF * q, :],
                                   w_hi[:, f, :], w_lo[:, f, :], f == 0, False)
                last.then_inc(e_used, 1)

            def gram(t, half):
                if half == 0:
                    pe.wait_ge(e_raw_ready, (t + 1) * NQ)
                if half == 1:
                    pe.wait_ge(g_lo_ready, 2 * t + 1)
                for g in range(HG):
                    if half == 0 and g == HG // 2 and t >= 1:
                        pe.wait_ge(y_ready, t)
                    b = SPG * (half * HG + g)
                    out = gram_ps[:, g * GSTEP:g * GSTEP + NF * SPG]
                    e = e_raw[:, t % 2, b:b + SPG, :]
                    last = nc.tensor.matmul(out, e.rearrange("p s f -> p (s f)"), e[:, :, 0:NF], start=True, stop=True)
                last.then_inc(gram_done, 1)

            def pairs_h1(t):
                pe.wait_ge(g_lo_ready, 2 * t + 2)
                for c in range(CI):
                    if t == 0:
                        pe.wait_ge(w_lo_ready, F + c + 1)
                    k = P if c < CI - 1 else K_LAST
                    last = product(h1_ps[t % 2][:, :], g_hi[0:k, c, :], g_lo[0:k, c, :],
                                   w_hi[0:k, F + c, :], w_lo[0:k, F + c, :], False, c == CI - 1)
                last.then_inc(h1_done, 1)

            def transpose_h1(t):
                pe.wait_ge(h1_ready, t + 1)
                for c in range(HC):
                    last = nc.tensor.transpose(h1T_ps[:, c * P:(c + 1) * P], h1[:, c * P:(c + 1) * P], ident[:, :])
                last.then_inc(h1_transposed, 1)

            def layer2(t):
                pe.wait_ge(h1T_ready, t + 1)
                if t == 0:
                    pe.wait_ge(small_loaded, 48)
                for m in range(MC):
                    for c in range(HC):
                        last = nc.tensor.matmul(h2_ps[:, m, :], w2[:, c, m * P:(m + 1) * P], h1T[:, c, :],
                                                start=c == 0, stop=c == HC - 1)
                last.then_inc(h2_done, 1)

            def layer3(t):
                pe.wait_ge(h2_ready, t + 1)
                for m in range(MC):
                    last = nc.tensor.matmul(y_ps, w3[:, m:m + 1], h2T[:, m, :], start=m == 0, stop=m == MC - 1)
                last.then_inc(y_done, 1)

            transposes(0, 0)
            for t in range(NT + 1):
                if t >= 1:
                    gram(t - 1, 0)
                    embeddings_h1(t - 1, 6)
                if t < NT:
                    transposes(t, 1)
                    embeddings_h1(t, 0)
                if t >= 1:
                    gram(t - 1, 1)
                if t < NT:
                    transposes(t, 2)
                    embeddings_h1(t, 1)
                    transposes(t, 3)
                    embeddings_h1(t, 2)
                if t >= 1:
                    pairs_h1(t - 1)
                if t < NT:
                    transposes(t, 4)
                    embeddings_h1(t, 3)
                    transposes(t, 5)
                if t >= 1:
                    transpose_h1(t - 1)
                if t < NT:
                    embeddings_h1(t, 4)
                    transposes(t, 6)
                if t >= 1:
                    layer2(t - 1)
                if t < NT:
                    embeddings_h1(t, 5)
                if t + 1 < NT:
                    transposes(t + 1, 0)
                if t >= 1:
                    layer3(t - 1)


_TABLES = [f"tbl_{f}" for f in range(27)]
_INS = ["dense_ctx", "ids"] + _TABLES + ["W_top1", "b_top1", "W_top2", "b_top2", "W_top3"]


def kernel(**inputs):
    import numpy as _np
    import concourse.bacc as _bacc
    from concourse import mybir as _mybir
    from concourse.bass_utils import run_bass_kernel_spmd as _run

    nc = _bacc.Bacc("TRN2", target_bir_lowering=False, num_devices=1, dynamic_dma_scratch_size=4096)
    arrays, aps = {}, {}
    for name in _INS:
        a = _np.ascontiguousarray(inputs[name])
        arrays[f"in_{name}"] = a
        aps[name] = nc.dram_tensor(f"in_{name}", a.shape, _mybir.dt.from_np(a.dtype), kind="ExternalInput").ap()
    y = nc.dram_tensor("out_y", (aps["ids"].shape[0], 1), _mybir.dt.from_np(_np.dtype("float32")),
                       kind="ExternalOutput").ap()
    dlrm_tower(nc, aps["dense_ctx"], aps["ids"], [aps[n] for n in _TABLES], aps["W_top1"], aps["b_top1"],
               aps["W_top2"], aps["b_top2"], aps["W_top3"], y)
    return _run(nc, [arrays], core_ids=[0]).results[0]["out_y"]
```

```python
import concourse.bass as bass
from concourse import mybir
from contextlib import ExitStack


def dlrm_tower(nc, dense_ctx, ids, tables, W_top1, b_top1, W_top2, b_top2, W_top3, y_out):
    f32, f32r, i32 = mybir.dt.float32, mybir.dt.float32r, mybir.dt.int32
    ALU = mybir.AluOpType
    ACT = mybir.ActivationFunctionType

    P = 128
    B, F = ids.shape
    D = tables[0].shape[1]
    CTX = dense_ctx.shape[1]
    H1, H2 = W_top2.shape
    NT = B // P
    QF = 4
    NQ = -(-F // QF)
    RING = 14
    SPG = 4
    ROWS = P // SPG
    FM = F + F % 2
    NG = P // SPG
    GP = 8
    PG = NG // GP
    GSTEP = 256
    CI = -(-(F + 1) // 4)
    CTX_AT = 3 * ROWS
    STAGE = 10
    PER_DMA = 2
    PAIR0 = F * D
    CTX0 = PAIR0 + F * (F - 1) // 2
    HC = H1 // P
    assert B == NT * P and D == P and CTX < ROWS and H1 == 512 and P + H2 <= H1 and F == 4 * CI - 1 and F <= ROWS

    def pair_row(f):
        return PAIR0 + f * (F - 1) - f * (f - 1) // 2

    def place(f):
        return divmod(f, CI)

    def quad_features(q):
        return range(QF * q, min(QF * q + QF, F))

    ctx = ExitStack()
    with ctx:
        def sb(name, shape, dt):
            return ctx.enter_context(nc.sbuf_tensor(name, shape, dt))

        def sem(name):
            return ctx.enter_context(nc.semaphore(name))

        w_hi = sb("w_hi", [P, F, H1], f32r)
        w_lo = sb("w_lo", [P, F, H1], f32r)
        w_pairs = sb("w_pairs", [P, CI, H1], f32)
        e = sb("e", [P, 2, 2, P, ROWS], f32r)
        wp = e[:, 0, :, :, :].rearrange("p h b f -> p h (b f)")[:, :, 0:CI * H1].rearrange(
            "p h (c n) -> p h c n", n=H1)
        x_hi = sb("x_hi", [P, CI, P], f32r)
        x_lo = sb("x_lo", [P, CI, P], f32r)
        rows = sb("rows", [P, RING, D], f32)
        stage = sb("stage", [P, STAGE, H1], f32)
        h1 = stage[:, 0, :]
        h1T = stage[:, 0, :].rearrange("p (c b) -> p c b", c=HC)
        w2 = stage[:, 1:3, :].rearrange("p a (c n) -> p (a c) n", n=H2)
        y = stage[:, 3:10, :].rearrange("p a n -> p (a n)").rearrange("p (g m) -> p g m", m=SPG * FM)
        x_first = stage[:, 0:2, :].rearrange("p a n -> p (a n)")[:, 0:CI * P].rearrange("p (c b) -> p c b", c=CI)
        x_later = w_pairs[:, :, 0:P]
        ids_sb = sb("ids_sb", [P, NT, F], i32)
        ctx_sb = sb("ctx_sb", [P, NT, CTX], f32)
        b2 = w_pairs[:, 0, P:P + H2]
        w3 = w_pairs[:, 1, P:P + H2]
        h2 = w_pairs[:, 2, P:P + H2]
        products = w_pairs[:, 3, P:P + H2]
        y_col = w_pairs[:, 4, P:P + 1]
        ident = sb("ident", [P, P], f32)

        h1_ps = [ctx.enter_context(nc.psum_tensor(f"h1_ps{i}", [P, H1], f32)) for i in range(2)]
        tp_ps = [ctx.enter_context(nc.psum_tensor(f"tp_ps{i}", [P, QF, P], f32)) for i in range(2)]
        gram_ps = ctx.enter_context(nc.psum_tensor("gram_ps", [P, 4 * 512], f32))
        h1T_ps = gram_ps[:, 0:1024].rearrange("p (h n) -> p h n", h=2)[:, :, 0:HC // 2 * P]
        h2_ps = gram_ps[:, 1024:1024 + H2]

        ids0_loaded = sem("ids0_loaded")
        ids_loaded = sem("ids_loaded")
        ctx_loaded = sem("ctx_loaded")
        ident_zeroed = sem("ident_zeroed")
        ident_ready = sem("ident_ready")
        pads_ready = sem("pads_ready")
        rows_landed = [sem(f"rows_landed{i}") for i in range(RING)]
        w_landed = [sem(f"w_landed{i}") for i in range(STAGE // PER_DMA)]
        pairs_zeroed = sem("pairs_zeroed")
        pairs_loaded = sem("pairs_loaded")
        w_hi_ready = sem("w_hi_ready")
        w_lo_ready = sem("w_lo_ready")
        small_loaded = sem("small_loaded")
        transposed = sem("transposed")
        e_hi_ready = sem("e_hi_ready")
        e_lo_ready = sem("e_lo_ready")
        gram_done = sem("gram_done")
        e_used = sem("e_used")
        half_a_ready = sem("half_a_ready")
        y_sum_ready = sem("y_sum_ready")
        x_zeroed = sem("x_zeroed")
        x_act_moved = sem("x_act_moved")
        x_dve_moved = sem("x_dve_moved")
        x_hi_ready = sem("x_hi_ready")
        x_lo_ready = sem("x_lo_ready")
        wp_hi_ready = sem("wp_hi_ready")
        wp_lo_ready = sem("wp_lo_ready")
        h1_done = sem("h1_done")
        h1_ready = sem("h1_ready")
        h1_transposed = sem("h1_transposed")
        h1T_dve_ready = sem("h1T_dve_ready")
        h1T_act_ready = sem("h1T_act_ready")
        h2_done = sem("h2_done")
        h2_ready = sem("h2_ready")
        y_ready = sem("y_ready")
        y_stored = sem("y_stored")

        def tile_e(part, t, f0, f1):
            return e[:, min(t, 1), part, :, f0:f1].rearrange("p b f -> p f b")

        def w_sem(c):
            return w_landed[c % STAGE // PER_DMA]

        def w_count(c):
            return 16 * (c // STAGE + 1)

        def gram_view(part, b):
            banks = gram_ps[:, part % 2 * PG * GSTEP:(part % 2 + 1) * PG * GSTEP]
            return banks.rearrange("p (g m) -> p g m", m=GSTEP)[:, :, b * SPG * FM:(b + 1) * SPG * FM]

        def moves(t, half, s):
            x = x_first if t == 0 else x_later
            gs = slice(half * NG // 2, (half + 1) * NG // 2)
            for q in range(4):
                n = min(CI, F - CI * q)
                to = x[ROWS * q:ROWS * q + F, 0:n, :].rearrange("p c (g s) -> p c g s", s=SPG)
                at = s * FM + CI * q
                yield to[:, :, gs, s], y[ROWS * s:ROWS * s + F, gs, at:at + n].rearrange("p g c -> p c g")

        def pair_weight_loads():
            for f in range(F - 1):
                q, c = place(f)
                yield w_pairs[ROWS * q + f + 1:ROWS * q + F, c, :], W_top1[pair_row(f):pair_row(f) + F - 1 - f, :]
            for q in range(4):
                f = 0
                while f < min(CI * (q + 1), F) - 1:
                    g0, g1 = max(CI * q, f + 1), min(CI * (q + 1), F)
                    c = place(g0)[1]
                    at = pair_row(f) + g0 - f - 1
                    if f + 1 < g0 and f + 2 < CI * q + 1:
                        step = pair_row(f + 1) - pair_row(f) - 1
                        src = W_top1[at:at + 2 * step, :].rearrange("(a c) n -> a c n", a=2)[:, 0:g1 - g0, :]
                        yield w_pairs[ROWS * q + f:ROWS * q + f + 2, c:c + g1 - g0, :], src
                        f += 2
                    else:
                        src = W_top1[at:at + g1 - g0, :].rearrange("(a c) n -> a c n", a=1)
                        yield w_pairs[ROWS * q + f:ROWS * q + f + 1, c:c + g1 - g0, :], src
                        f += 1
            yield w_pairs[CTX_AT:CTX_AT + CTX, CI - 1, :], W_top1[CTX0:CTX0 + CTX, :]
            yield w_pairs[CTX_AT + CTX:CTX_AT + CTX + 1, CI - 1, :], b_top1.rearrange("(a n) -> a n", a=1)

        X_RUNS = [(P, 0, 3), (P, 3, CI - 1), (CTX_AT, CI - 1, CI)]
        NR = len(X_RUNS)

        def run_of(t, x, run):
            partitions, c0, c1 = run
            x = x if x is not None else x_first if t == 0 else x_later
            return x[0:partitions, c0:c1, :]

        N_PAIR_LOADS = len(list(pair_weight_loads()))

        block = ctx.enter_context(nc.Block())

        @block.sync
        def _(sp):
            ids_v = ids.rearrange("(t p) f -> p t f", p=P)
            sp.dma_start(ids_sb[:, 0, :], ids_v[:, 0, :]).then_inc(ids0_loaded, 16)
            pair_loads = list(pair_weight_loads())
            n_pair_loads = len(pair_loads)
            for c in range(0, F, PER_DMA):
                n = min(PER_DMA, F - c)
                if c >= STAGE:
                    sp.wait_ge(w_lo_ready, c + n - STAGE)
                elif c >= 4:
                    sp.wait_ge(rows_landed[c - 4], 16)
                sp.dma_start(stage[:, c % STAGE:c % STAGE + n, :],
                             W_top1[c * D:(c + n) * D, :].rearrange("(c p) n -> p c n", p=P)).then_inc(w_sem(c), 16)
                if c == 0:
                    sp.dma_start(ids_sb[:, 1:NT, :], ids_v[:, 1:NT, :]).then_inc(ids_loaded, 16)
                    sp.dma_start(ctx_sb[:, :, :], dense_ctx.rearrange("(t p) f -> p t f", p=P)).then_inc(ctx_loaded, 16)
                if c >= STAGE - PER_DMA:
                    if c == STAGE - PER_DMA:
                        sp.wait_ge(pairs_zeroed, 1)
                    for _ in range(3):
                        dst, src = pair_loads.pop(0)
                        sp.dma_start(dst, src).then_inc(pairs_loaded, 16)
            for dst, src in pair_loads:
                sp.dma_start(dst, src).then_inc(pairs_loaded, 16)
            assert n_pair_loads == N_PAIR_LOADS
            sp.wait_ge(x_lo_ready, NR)
            sp.dma_start(w2, W_top2.rearrange("(c p) n -> p c n", p=P)).then_inc(small_loaded, 16)
            sp.wait_ge(wp_lo_ready, CI)
            sp.dma_start(b2, b_top2.rearrange("(a n) -> a n", a=1).broadcast_to([P, H2])).then_inc(small_loaded, 16)
            sp.dma_start(w3, W_top3.rearrange("n o -> o n").broadcast_to([P, H2])).then_inc(small_loaded, 16)
            for t in range(NT):
                sp.wait_ge(y_ready, t + 1)
                sp.dma_start(y_out[t * P:(t + 1) * P, :], y_col).then_inc(y_stored, 16)
            sp.wait_ge(y_stored, 16 * NT)

        @block.gpsimd
        def _(pool):
            nc.gpsimd.memset(ident[:, :], 0.0).then_inc(ident_zeroed, 1)
            pool.wait_ge(ident_zeroed, 1)
            nc.gpsimd.affine_select(out=ident[:, :], in_=ident[:, :], compare_op=ALU.not_equal, fill=1.0,
                                    base=0, pattern=[[-1, P]], channel_multiplier=1).then_inc(ident_ready, 1)
            for k in range(NT * NQ):
                t, q = divmod(k, NQ)
                if k == 0:
                    pool.wait_ge(ids0_loaded, 16)
                if k == NQ:
                    pool.wait_ge(ids_loaded, 16)
                for f in quad_features(q):
                    n = t * F + f
                    if n >= RING:
                        old_t, old_f = divmod(n - RING, F)
                        pool.wait_ge(transposed, old_t * NQ + old_f // QF + 1)
                    nc.gpsimd.indirect_dma_start(
                        rows[:, n % RING, :], None, tables[f],
                        bass.IndirectOffsetOnAxis(ids_sb[:, t, f:f + 1], 0)).then_inc(rows_landed[n % RING], 16)

        @block.scalar
        def _(act):
            def split_w(c):
                act.wait_ge(w_sem(c), w_count(c))
                nc.scalar.activation(w_hi[:, c, :], stage[:, c % STAGE, :], ACT.Copy).then_inc(w_hi_ready, 1)

            def split_e(t, q):
                k = t * NQ + q
                fs = quad_features(q)
                if t == 0:
                    for c in fs:
                        split_w(c)
                if t >= 2:
                    act.wait_ge(e_used, k - NQ + 1)
                    if q == 0:
                        act.wait_ge(gram_done, GP * t)
                act.wait_ge(transposed, k + 1)
                last = nc.scalar.activation(tile_e(0, t, fs[0], fs[-1] + 1), tp_ps[k % 2][:, 0:len(fs), :], ACT.Copy)
                if q == NQ - 1:
                    if t == 0:
                        act.wait_ge(pads_ready, 7)
                    else:
                        act.wait_ge(h1_done, t)
                    last = nc.scalar.activation(x_hi[CTX_AT:CTX_AT + CTX, CI - 1, :],
                                                tp_ps[k % 2][0:CTX, QF - 1, :], ACT.Copy)
                last.then_inc(e_hi_ready, 1)

            def half_a(t, part):
                act.wait_ge(gram_done, GP * t + part + 1)
                if part == 0 and t == 0:
                    act.wait_ge(w_lo_ready, F)
                if part == 0 and t >= 1:
                    act.wait_ge(x_dve_moved, t)
                nc.scalar.activation(y[:, part * PG:(part + 1) * PG, :], gram_view(part, 0), ACT.Copy,
                                     scale=0.5).then_inc(half_a_ready, 1)

            def move_x(t, half, s):
                act.wait_ge(y_sum_ready, GP * t + GP // 2 * (half + 1))
                if t == 0:
                    act.wait_ge(x_zeroed, 1)
                if t == 1:
                    act.wait_ge(wp_lo_ready, CI)
                if t >= 2:
                    act.wait_ge(x_lo_ready, NR * t)
                for dst, src in moves(t, half, s):
                    last = nc.scalar.activation(dst, src, ACT.Copy)
                if half == 1 and s == 1:
                    last.then_inc(x_act_moved, 1)

            def split_x(t):
                act.wait_ge(x_act_moved, t + 1)
                act.wait_ge(x_dve_moved, t + 1)
                if t >= 1:
                    act.wait_ge(h1_done, t)
                for run in X_RUNS:
                    nc.scalar.activation(run_of(t, x_hi, run), run_of(t, None, run), ACT.Copy).then_inc(x_hi_ready, 1)

            def split_wp():
                act.wait_ge(gram_done, GP)
                act.wait_ge(e_used, NQ)
                act.wait_ge(pairs_loaded, 16 * N_PAIR_LOADS)
                for c in range(CI):
                    nc.scalar.activation(wp[:, 0, c, :], w_pairs[:, c, :], ACT.Copy).then_inc(wp_hi_ready, 1)

            def relu_h1(t):
                act.wait_ge(h1_done, t + 1)
                if t == 0:
                    act.wait_ge(w_lo_ready, F)
                else:
                    act.wait_ge(h2_done, t)
                for half in range(2):
                    cols = slice(half * H1 // 2, (half + 1) * H1 // 2)
                    nc.scalar.activation(h1[:, cols], h1_ps[t % 2][:, cols], ACT.Relu).then_inc(h1_ready, 1)

            def copy_h1T(t):
                act.wait_ge(h1_transposed, 2 * t + 2)
                nc.scalar.activation(h1T[:, HC // 2:HC, :].rearrange("p c b -> p (c b)"), h1T_ps[:, 1, :],
                                     ACT.Copy).then_inc(h1T_act_ready, 1)

            def sums(t, first, end):
                for part in range(first, end):
                    half_a(t, part)

            for q in range(NQ):
                split_e(0, q)
            sums(0, 0, 2)
            split_e(1, 0)
            sums(0, 2, 5)
            split_e(1, 1)
            move_x(0, 0, 0)
            sums(0, 5, 6)
            split_e(1, 2)
            move_x(0, 0, 1)
            sums(0, 6, 8)
            split_e(1, 3)
            move_x(0, 1, 0)
            move_x(0, 1, 1)
            split_x(0)
            split_wp()
            split_e(1, 4)
            relu_h1(0)
            split_e(1, 5)
            copy_h1T(0)
            split_e(1, 6)
            for t in range(1, NT):
                sums(t, 0, 5)
                move_x(t, 0, 0)
                sums(t, 5, 6)
                move_x(t, 0, 1)
                sums(t, 6, 7)
                if t + 1 < NT:
                    split_e(t + 1, 0)
                sums(t, 7, 8)
                move_x(t, 1, 0)
                move_x(t, 1, 1)
                split_x(t)
                if t + 1 < NT:
                    split_e(t + 1, 1)
                    split_e(t + 1, 2)
                    relu_h1(t)
                    split_e(t + 1, 3)
                    copy_h1T(t)
                    split_e(t + 1, 4)
                    split_e(t + 1, 5)
                    split_e(t + 1, 6)
            relu_h1(NT - 1)
            copy_h1T(NT - 1)

        @block.vector
        def _(dve):
            def split_w(c):
                dve.wait_ge(w_hi_ready, c + 1)
                nc.vector.tensor_tensor(w_lo[:, c, :], stage[:, c % STAGE, :], w_hi[:, c, :],
                                        ALU.subtract).then_inc(w_lo_ready, 1)

            def split_e(t, q):
                k = t * NQ + q
                fs = quad_features(q)
                if t == 0 and q >= 1:
                    for c in fs:
                        split_w(c)
                dve.wait_ge(e_hi_ready, k + 1)
                last = nc.vector.tensor_tensor(tile_e(1, t, fs[0], fs[-1] + 1), tp_ps[k % 2][:, 0:len(fs), :],
                                               tile_e(0, t, fs[0], fs[-1] + 1), ALU.subtract)
                if q == NQ - 1:
                    last = nc.vector.tensor_tensor(x_lo[CTX_AT:CTX_AT + CTX, CI - 1, :],
                                                   tp_ps[k % 2][0:CTX, QF - 1, :],
                                                   x_hi[CTX_AT:CTX_AT + CTX, CI - 1, :], ALU.subtract)
                last.then_inc(e_lo_ready, 1)

            def add_b(t, part):
                dve.wait_ge(half_a_ready, GP * t + part + 1)
                sums = y[:, part * PG:(part + 1) * PG, :]
                nc.vector.tensor_tensor(sums, sums, gram_view(part, 1), ALU.add).then_inc(y_sum_ready, 1)

            def move_x(t, half, s):
                dve.wait_ge(y_sum_ready, GP * t + GP // 2 * (half + 1))
                if t == 0:
                    dve.wait_ge(x_zeroed, 1)
                if t == 1:
                    dve.wait_ge(wp_lo_ready, CI)
                if t >= 2:
                    dve.wait_ge(x_lo_ready, NR * t)
                for dst, src in moves(t, half, s):
                    last = nc.vector.tensor_copy(dst, src)
                if half == 1 and s == 3:
                    last.then_inc(x_dve_moved, 1)

            def split_x(t):
                for i, run in enumerate(X_RUNS):
                    dve.wait_ge(x_hi_ready, NR * t + i + 1)
                    nc.vector.tensor_tensor(run_of(t, x_lo, run), run_of(t, None, run), run_of(t, x_hi, run),
                                            ALU.subtract).then_inc(x_lo_ready, 1)

            def split_wp():
                for c in range(CI):
                    dve.wait_ge(wp_hi_ready, c + 1)
                    nc.vector.tensor_tensor(wp[:, 1, c, :], w_pairs[:, c, :], wp[:, 0, c, :],
                                            ALU.subtract).then_inc(wp_lo_ready, 1)

            def copy_h1T(t):
                dve.wait_ge(h1_transposed, 2 * t + 1)
                nc.vector.tensor_copy(h1T[:, 0:HC // 2, :].rearrange("p c b -> p (c b)"),
                                      h1T_ps[:, 0, :]).then_inc(h1T_dve_ready, 1)

            def finish_y(t):
                dve.wait_ge(h2_done, t + 1)
                if t == 0:
                    dve.wait_ge(small_loaded, 48)
                nc.vector.tensor_tensor(h2, h2_ps, b2, ALU.add).then_inc(h2_ready, 1)
                dve.wait_ge(h2_ready, t + 1)
                if t >= 1:
                    dve.wait_ge(y_stored, 16 * t)
                nc.vector.scalar_tensor_tensor(products, h2, 0.0, w3, ALU.max, ALU.mult,
                                               accum_out=y_col).then_inc(y_ready, 1)

            def sums(t, first, end):
                for part in range(first, end):
                    add_b(t, part)

            def zero_unused():
                for i in range(2):
                    for part in range(2):
                        nc.vector.memset(e[:, i, part, :, F:ROWS].bitcast(f32), 0.0).then_inc(pads_ready, 1)
                for x in (x_hi, x_lo):
                    nc.vector.memset(x[:, :, :].bitcast(f32), 0.0).then_inc(pads_ready, 1)
                dve.wait_ge(pads_ready, 6)
                nc.vector.memset(x_hi[CTX_AT:P, CI - 1, :].bitcast(f32), 1.0).then_inc(pads_ready, 1)

            nc.vector.memset(w_pairs[:, :, :], 0.0).then_inc(pairs_zeroed, 1)
            for c in quad_features(0):
                split_w(c)
            zero_unused()
            for q in range(NQ):
                split_e(0, q)
            dve.wait_ge(w_lo_ready, F)
            nc.vector.memset(x_first, 0.0).then_inc(x_zeroed, 1)
            sums(0, 0, 2)
            split_e(1, 0)
            sums(0, 2, 5)
            split_e(1, 1)
            move_x(0, 0, 2)
            sums(0, 5, 6)
            split_e(1, 2)
            move_x(0, 0, 3)
            sums(0, 6, 8)
            split_e(1, 3)
            move_x(0, 1, 2)
            move_x(0, 1, 3)
            split_x(0)
            split_wp()
            split_e(1, 4)
            split_e(1, 5)
            copy_h1T(0)
            split_e(1, 6)
            for t in range(1, NT):
                if t == 1:
                    finish_y(0)
                sums(t, 0, 5)
                move_x(t, 0, 2)
                sums(t, 5, 6)
                move_x(t, 0, 3)
                sums(t, 6, 7)
                if t + 1 < NT:
                    split_e(t + 1, 0)
                sums(t, 7, 8)
                move_x(t, 1, 2)
                move_x(t, 1, 3)
                split_x(t)
                if t + 1 < NT:
                    split_e(t + 1, 1)
                    split_e(t + 1, 2)
                    split_e(t + 1, 3)
                    copy_h1T(t)
                    split_e(t + 1, 4)
                    finish_y(t)
                    split_e(t + 1, 5)
                    split_e(t + 1, 6)
            copy_h1T(NT - 1)
            finish_y(NT - 1)

        @block.tensor
        def _(pe):
            def transposes(t, q, first=0, end=QF):
                k = t * NQ + q
                if k == 0:
                    pe.wait_ge(ident_ready, 1)
                if k >= 2 and first == 0:
                    pe.wait_ge(e_lo_ready, k - 1)
                for i, f in list(enumerate(quad_features(q)))[first:end]:
                    n = t * F + f
                    pe.wait_ge(rows_landed[n % RING], 16 * (n // RING + 1))
                    last = nc.tensor.transpose(tp_ps[k % 2][:, i, :], rows[:, n % RING, :], ident[:, :])
                if end < QF:
                    return
                if q == NQ - 1:
                    if t == 0:
                        pe.wait_ge(ctx_loaded, 16)
                    last = nc.tensor.transpose(tp_ps[k % 2][0:CTX, QF - 1, :], ctx_sb[:, t, :], ident[:, :])
                last.then_inc(transposed, 1)

            def embeddings_h1(t, q, first=0, end=QF):
                if q == 0 and first == 0 and t >= 2:
                    pe.wait_ge(h1_ready, 2 * (t - 1))
                pe.wait_ge(e_lo_ready, t * NQ + q + 1)
                for f in quad_features(q)[first:end]:
                    if t == 0:
                        pe.wait_ge(w_lo_ready, f + 1)
                    out, hi, lo = h1_ps[t % 2][:, :], tile_e(0, t, f, f + 1)[:, 0, :], tile_e(1, t, f, f + 1)[:, 0, :]
                    nc.tensor.matmul(out, hi, w_hi[:, f, :], start=f == 0, stop=False)
                    nc.tensor.matmul(out, hi, w_lo[:, f, :], start=False, stop=False)
                    last = nc.tensor.matmul(out, lo, w_hi[:, f, :], start=False, stop=False)
                    if f == quad_features(q)[-1]:
                        last.then_inc(e_used, 1)

            def gram(t, part):
                if part == 0:
                    pe.wait_ge(e_lo_ready, (t + 1) * NQ)
                    if t == 0:
                        pe.wait_ge(pads_ready, 7)
                if part == 1 and t >= 1:
                    pe.wait_ge(h2_ready, t)
                if part >= 2:
                    pe.wait_ge(y_sum_ready, GP * t + part - 1)
                for g in range(PG):
                    b = SPG * (part * PG + g)
                    at = (part % 2 * PG + g) * GSTEP
                    pair = e[:, min(t, 1), :, b:b + SPG, :]
                    last = nc.tensor.matmul(gram_ps[:, at:at + 2 * SPG * FM],
                                            pair[:, 0, :, :].rearrange("p s f -> p (s f)"),
                                            pair[:, :, :, 0:FM], start=True, stop=True)
                last.then_inc(gram_done, 1)

            def pairs_h1(t):
                for c in range(CI):
                    for i, (_, first, _) in enumerate(X_RUNS):
                        if c == first:
                            pe.wait_ge(x_lo_ready, NR * t + i + 1)
                    if t == 0:
                        pe.wait_ge(wp_lo_ready, c + 1)
                    out = h1_ps[t % 2][:, :]
                    nc.tensor.matmul(out, x_hi[:, c, :], wp[:, 0, c, :], start=False, stop=False)
                    nc.tensor.matmul(out, x_hi[:, c, :], wp[:, 1, c, :], start=False, stop=False)
                    last = nc.tensor.matmul(out, x_lo[:, c, :], wp[:, 0, c, :], start=False, stop=c == CI - 1)
                last.then_inc(h1_done, 1)

            def transpose_h1(t):
                for half in range(2):
                    pe.wait_ge(h1_ready, 2 * t + half + 1)
                    for i in range(HC // 2):
                        c = half * HC // 2 + i
                        last = nc.tensor.transpose(h1T_ps[:, half, i * P:(i + 1) * P], h1[:, c * P:(c + 1) * P],
                                                   ident[:, :])
                    last.then_inc(h1_transposed, 1)

            def layer2(t):
                if t == 0:
                    pe.wait_ge(small_loaded, 48)
                for c in range(HC):
                    if c == 0:
                        pe.wait_ge(h1T_dve_ready, t + 1)
                    if c == HC // 2:
                        pe.wait_ge(h1T_act_ready, t + 1)
                    last = nc.tensor.matmul(h2_ps, h1T[:, c, :], w2[:, c, :], start=c == 0, stop=c == HC - 1)
                last.then_inc(h2_done, 1)

            def grams(t, f):
                gram(t, 0)
                for part in range(1, GP):
                    embeddings_h1(t, f // QF, f % QF, f % QF + 1)
                    f += 1
                    if part == 6 and t + 1 < NT:
                        transposes(t + 1, 0)
                    gram(t, part)
                for f in range(f, F):
                    embeddings_h1(t, f // QF, f % QF, f % QF + 1)
                if t + 1 < NT:
                    transposes(t + 1, 1)
                    embeddings_h1(t + 1, 0)
                    transposes(t + 1, 2)

            transposes(0, 0)
            for q in range(NQ - 1):
                if q < 3:
                    transposes(0, q + 1)
                    embeddings_h1(0, q)
                else:
                    transposes(0, q + 1, 0, 2)
                    embeddings_h1(0, q, 0, 1)
                    transposes(0, q + 1, 2, 3)
                    embeddings_h1(0, q, 1, 2)
                    transposes(0, q + 1, 3)
                    embeddings_h1(0, q, 2)
            gram(0, 0)
            gram(0, 1)
            embeddings_h1(0, 6, 0, 1)
            transposes(1, 0)
            gram(0, 2)
            embeddings_h1(0, 6, 1, 2)
            gram(0, 3)
            embeddings_h1(0, 6, 2)
            gram(0, 4)
            transposes(1, 1)
            embeddings_h1(1, 0, 0, 2)
            gram(0, 5)
            embeddings_h1(1, 0, 2)
            gram(0, 6)
            transposes(1, 2)
            embeddings_h1(1, 1, 0, 2)
            gram(0, 7)
            embeddings_h1(1, 1, 2)
            embeddings_h1(1, 2, 0, 1)
            transposes(1, 3)
            embeddings_h1(1, 2, 1)
            embeddings_h1(1, 3, 0, 3)
            transposes(1, 4)
            embeddings_h1(1, 3, 3)
            pairs_h1(0)
            transposes(1, 5)
            embeddings_h1(1, 4, 0, 1)
            transpose_h1(0)
            transposes(1, 6)
            embeddings_h1(1, 4, 1, 2)
            layer2(0)
            grams(1, 18)
            for t in range(2, NT):
                pairs_h1(t - 1)
                embeddings_h1(t, 1, 0, 2)
                transposes(t, 3)
                transpose_h1(t - 1)
                embeddings_h1(t, 1, 2)
                transposes(t, 4)
                layer2(t - 1)
                transposes(t, 5)
                embeddings_h1(t, 2, 0, 2)
                transposes(t, 6)
                embeddings_h1(t, 2, 2)
                embeddings_h1(t, 3, 0, QF if t + 1 < NT else 1)
                grams(t, 16 if t + 1 < NT else 13)
            pairs_h1(NT - 1)
            transpose_h1(NT - 1)
            layer2(NT - 1)


_TABLES = [f"tbl_{f}" for f in range(27)]
_INS = ["dense_ctx", "ids"] + _TABLES + ["W_top1", "b_top1", "W_top2", "b_top2", "W_top3"]


def kernel(**inputs):
    import numpy as _np
    import concourse.bacc as _bacc
    from concourse import mybir as _mybir
    from concourse.bass_utils import run_bass_kernel_spmd as _run

    nc = _bacc.Bacc("TRN2", target_bir_lowering=False, num_devices=1, dynamic_dma_scratch_size=2048)
    arrays, aps = {}, {}
    for name in _INS:
        a = _np.ascontiguousarray(inputs[name])
        arrays[f"in_{name}"] = a
        aps[name] = nc.dram_tensor(f"in_{name}", a.shape, _mybir.dt.from_np(a.dtype), kind="ExternalInput").ap()
    y = nc.dram_tensor("out_y", (aps["ids"].shape[0], 1), _mybir.dt.from_np(_np.dtype("float32")),
                       kind="ExternalOutput").ap()
    dlrm_tower(nc, aps["dense_ctx"], aps["ids"], [aps[n] for n in _TABLES], aps["W_top1"], aps["b_top1"],
               aps["W_top2"], aps["b_top2"], aps["W_top3"], y)
    return _run(nc, [arrays], core_ids=[0]).results[0]["out_y"]
```
